# Optimizing a Trainium2 kernel written in Bass

```python
import numpy as np
import jax
import jax.numpy as jnp

def _softmax(x, axis=-1):
    return jax.nn.softmax(x, axis=axis)

def _gelu(x):
    return jax.nn.gelu(x, approximate=True)

def _silu(x):
    return jax.nn.silu(x)

def _sigmoid(x):
    return jax.nn.sigmoid(x)

def _layernorm(x, axis=-1, eps=1e-05):
    m = jnp.mean(x, axis=axis, keepdims=True)
    v = jnp.var(x, axis=axis, keepdims=True)
    return (x - m) / jnp.sqrt(v + eps)

def _scatter_add(tgt, idx, src, axis=0):
    return tgt.at[idx].add(src)

def _segment_sum(src, seg, n):
    return jax.ops.segment_sum(src, seg, n)
kernel_name = 'mk_cond_resid_d2_seqx_r2_be1dff'

def setup_inputs(seed: int=0):
    np.random.seed(seed)
    _w = jnp.asarray

    def _rec_inputs():
        import jax
        import jax.numpy as jnp
        _rk = jax.random.key(seed)
        x = -7.109e-05 + 0.9999 * jax.random.normal(jax.random.fold_in(_rk, 1), (64, 128, 2048), jnp.float32)
        _lenS = 128 - jax.random.randint(jax.random.fold_in(_rk, 7), (64,), 0, max(1, 128 // 4) + 1, jnp.int32)
        _lenS2 = 128 - jax.random.randint(jax.random.fold_in(_rk, 8), (64,), 0, max(1, 128 // 4) + 1, jnp.int32)
        itok_B_0_15 = jax.random.randint(jax.random.fold_in(_rk, 11), (64,), 0, 16, jnp.int32)
        itok_B_4_50 = jax.random.randint(jax.random.fold_in(_rk, 12), (64,), 4, 51, jnp.int32)
        return (x, itok_B_0_15, itok_B_4_50)
    x, itok_B_0_15, itok_B_4_50 = _rec_inputs()

    def _L0_cond_setup():
        import jax, jax.numpy as jnp
        import numpy as np
        B, C, T = (64, 128, 2048)
        S, D = (16, 128)
        key = jax.random.key(seed)
        k1, k2, k3 = jax.random.split(key, 3)
        x = jax.random.normal(k1, (B, C, T), dtype=jnp.float32)
        condition = jax.random.randint(k2, (B,), 0, S, dtype=jnp.int64)
        bound = float(np.sqrt(6.0 / C))
        weights = jax.random.uniform(k3, (S, C, D), dtype=jnp.float32, minval=-bound, maxval=bound)
        return {'x': x, 'condition': condition, 'weights': weights}
    _L0_cond_all = _L0_cond_setup()
    _L0_cond_in = {k: v for k, v in _L0_cond_all.items() if k in ('weights',)}
    del _L0_cond_all

    def _L1_cond_setup():
        import jax, jax.numpy as jnp
        import numpy as np
        RANK = 16
        ALPHA = 16.0
        SCALING = ALPHA / RANK
        key = jax.random.key(seed)
        k1, k2, k3, k4 = jax.random.split(key, 4)
        batch, n_tok, d_in, d_out, n_adapters, rank = (8, 1024, 2048, 2048, 64, RANK)
        x = jax.random.normal(k1, (batch, n_tok, d_in), dtype=jnp.float32)
        A = jax.random.normal(k2, (n_adapters, d_out, rank), dtype=jnp.float32) * 0.02
        B = jax.random.normal(k3, (n_adapters, rank, d_in), dtype=jnp.float32)
        adapter_ids = jax.random.randint(k4, (batch,), 0, n_adapters, dtype=jnp.int32)
        return {'x': x, 'A': A, 'B': B, 'adapter_ids': adapter_ids}
    _L1_cond_all = _L1_cond_setup()
    _L1_cond_in = {k: v for k, v in _L1_cond_all.items() if k in ('A', 'B')}
    del _L1_cond_all
    return {'x': x, 'itok_B_0_15': itok_B_0_15, 'itok_B_4_50': itok_B_4_50, 'L0_cond_weights': _L0_cond_in['weights'], 'L1_cond_A': _L1_cond_in['A'], 'L1_cond_B': _L1_cond_in['B']}

def reference(x, itok_B_0_15, itok_B_4_50, L0_cond_weights, L1_cond_A, L1_cond_B):
    import jax
    import jax.numpy as jnp

    def _L0_cond_ref(x, condition, weights):
        import jax, jax.numpy as jnp
        import numpy as np
        B, C, T = (64, 128, 2048)
        S, D = (16, 128)
        W = weights[condition]
        return jnp.einsum('bct,bcd->bdt', x, W)

    def _L1_cond_ref(x, A, B, adapter_ids):
        import jax, jax.numpy as jnp
        import numpy as np
        RANK = 16
        ALPHA = 16.0
        SCALING = ALPHA / RANK
        B_req = B[adapter_ids]
        A_req = A[adapter_ids]
        Bx = jnp.einsum('bni,bri->bnr', x, B_req)
        out = jnp.einsum('bnr,bor->bno', Bx, A_req)
        return out * SCALING
    x = x + _L0_cond_ref(x, itok_B_0_15, L0_cond_weights)
    x = x + _L1_cond_ref(x, L1_cond_A, L1_cond_B, itok_B_4_50)
    return x

_drawn_inputs = setup_inputs


def setup_inputs(seed=0):
    import zlib

    import numpy as np

    out = dict(_drawn_inputs(seed))
    spreads = {}
    factors = {}
    for name, (base, spread) in spreads.items():
        noise = np.random.default_rng([zlib.crc32(name.encode()), seed]).standard_normal(out[name].shape)
        drawn = base * np.exp(spread * noise) if base else spread * noise
        out[name] = jnp.asarray(drawn.astype(out[name].dtype))
    for name, factor in factors.items():
        out[name] = (out[name] * factor).astype(out[name].dtype)
    return out
```

```python
from contextlib import ExitStack

import concourse.bass as bass
from concourse import mybir

F32 = mybir.dt.float32
BF16 = mybir.dt.bfloat16
I32 = mybir.dt.int32
ALU = mybir.AluOpType
ACT = mybir.ActivationFunctionType
AX = mybir.AxisListType

P = 128
GROUPS = 4
SLOTS = 4
BX_PARTS = 3
KSLOTS = 8
NPART = KSLOTS + BX_PARTS


def build(nc, x, cond, adapter, w, ab, out):
    BATCHES, C, T = x.shape
    EXPERTS = w.shape[1]
    ADAPTERS = ab.shape[0]
    CHUNKS = T // P
    R = ab.shape[2] // (2 * CHUNKS)
    CPG = CHUNKS // GROUPS
    GW = CPG * P
    BLOCKS = BATCHES // SLOTS
    assert C == P and KSLOTS * R == P and GW * 4 == 2048 and BATCHES % SLOTS == 0

    with ExitStack() as ctx:
        def sb(name, shape, dt):
            return ctx.enter_context(nc.sbuf_tensor(name, shape, dt))

        def psum(name, shape, dt):
            return ctx.enter_context(nc.psum_tensor(name, shape, dt))

        def sem(name):
            return ctx.enter_context(nc.semaphore(name))

        ids_cond = sb("ids_cond", [1, BATCHES], I32)
        ids_adapter = sb("ids_adapter", [1, BATCHES], I32)
        w_table = sb("w_table", [P, EXPERTS * C], F32)
        ident_f32 = sb("ident_f32", [P, P], F32)
        ident_bf16 = sb("ident_bf16", [P, P], BF16)
        x_sb = [sb(f"x_sb{s}", [P, T], F32) for s in range(SLOTS)]
        ab_sb = [sb(f"ab_sb{s}", [P, 2, CHUNKS, R], F32) for s in range(SLOTS)]
        y_sb = [sb(f"y_sb{s}", [P, T], F32) for s in range(SLOTS)]
        z_sb = [sb(f"z_sb{s}", [P, T], F32) for s in range(SLOTS)]
        w_sel = [sb(f"w_sel{s}", [P, C], F32) for s in range(2)]
        y_rem = [sb(f"y_rem{s}", [P, T], F32) for s in range(2)]
        y_part3 = [sb(f"y_part3{s}", [P, T], BF16) for s in range(2)]
        ab_parts = [sb(f"ab_parts{s}", [P, CHUNKS, NPART, R], BF16) for s in range(2)]
        ab_rem = sb("ab_rem", [P, 2, CHUNKS, R], F32)
        at_sb = [sb(f"at_sb{s}", [P, T], BF16) for s in range(2)]
        bx = sb("bx", [P, R], F32)
        bx_rem = sb("bx_rem", [P, R], F32)
        bx_parts = sb("bx_parts", [P, KSLOTS, R], BF16)
        bxt_sb = [sb(f"bxt_sb{s}", [P, P], BF16) for s in range(2)]

        y_ps = [psum(f"y_ps{s}", [P, GW], F32) for s in range(2)]
        z_ps = [psum(f"z_ps{s}", [P, GW], F32) for s in range(2)]
        at_ps = [psum(f"at_ps{s}", [P, 2 * GW], BF16) for s in range(2)]
        bx_ps = [psum(f"bx_ps{s}", [P, 512], F32) for s in range(2)]

        tables_loaded = sem("tables_loaded")
        ids_loaded = sem("ids_loaded")
        x_loaded = [sem(f"x_loaded{s}") for s in range(SLOTS)]
        ab_loaded = [sem(f"ab_loaded{s}") for s in range(SLOTS)]
        z_stored = [sem(f"z_stored{s}") for s in range(SLOTS)]
        zeroed = sem("zeroed")
        ident_ready = sem("ident_ready")
        w_ready = sem("w_ready")
        y_summed = sem("y_summed")
        y_copied = sem("y_copied")
        y_rem_ready = sem("y_rem_ready")
        y_part3_ready = sem("y_part3_ready")
        ab_part1 = sem("ab_part1")
        ab_rem_ready = sem("ab_rem_ready")
        ab_part2 = sem("ab_part2")
        ab_part3 = sem("ab_part3")
        a_slots_full = sem("a_slots_full")
        at_turned = sem("at_turned")
        at_copied = sem("at_copied")
        bx_summed = sem("bx_summed")
        bx_split = sem("bx_split")
        bxt_turned = sem("bxt_turned")
        bxt_copied = sem("bxt_copied")
        z_summed = sem("z_summed")
        z_ready = sem("z_ready")
        BX_OPS = 5

        def live(k):
            return not isinstance(k, int) or 0 <= k < BATCHES

        def wait(eng, semaphore, value):
            if not isinstance(value, int) or value > 0:
                eng.wait_ge(semaphore, value)

        def turn(q, u, lag):
            return q - 1 if u < lag else q

        def steps(eng, step, first_block, end_block, last):
            for k in range(SLOTS * first_block):
                step(k, k // SLOTS, k % SLOTS)
            with eng.Fori(first_block, end_block) as q:
                for u in range(SLOTS):
                    step(q * SLOTS + u, q, u)
            for k in range(SLOTS * end_block, last + 1):
                step(k, k // SLOTS, k % SLOTS)

        LAST = BATCHES + 1

        block = ctx.enter_context(nc.Block())

        @block.sync
        def _(sp):
            def load(b, s):
                sp.dma_start(x_sb[s][:, :], x[bass.ds(b, 1)].rearrange("o c t -> (o c) t")).then_inc(x_loaded[s], 16)
                a = sp.value_load(ids_adapter[0:1, bass.ds(b, 1)], min_val=0, max_val=ADAPTERS - 1)
                sp.dma_start(ab_sb[s][:, :, :, :].rearrange("p m j r -> p (m j r)"),
                             ab[bass.ds(a, 1)].rearrange("o p f -> (o p) f")).then_inc(ab_loaded[s], 16)

            sp.dma_start(ids_adapter[:, :], adapter).then_inc(ids_loaded, 16)
            sp.dma_start(ids_cond[:, :], cond).then_inc(ids_loaded, 16)
            sp.dma_start(w_table[:, :], w.rearrange("c e d -> c (e d)")).then_inc(tables_loaded, 16)
            sp.wait_ge(ids_loaded, 32)
            for b in range(SLOTS):
                load(b, b)

            def step(k, q, u):
                if live(k) and (not isinstance(k, int) or live(k + SLOTS)):
                    sp.wait_ge(y_summed, (k + 1) * GROUPS)
                    sp.wait_ge(ab_rem_ready, k + 1)
                    sp.wait_ge(ab_part1, k + 1)
                    load(k + SLOTS, u)
                if live(k - 2):
                    s = (u - 2) % SLOTS
                    sp.wait_ge(z_ready, (k - 1) * GROUPS)
                    sp.dma_start(out[bass.ds(k - 2, 1)].rearrange("o p f -> (o p) f"),
                                 z_sb[s][:, :]).then_inc(z_stored[s], 16)

            steps(sp, step, 1, BLOCKS - 1, LAST)
            for s in range(SLOTS):
                sp.wait_ge(z_stored[s], 16 * BLOCKS)

        @block.tensor
        def _(pe):
            def project(k, u, g):
                bank, m = bx_ps[(u - 1) % 2], (u - 1) % 2
                if g == 0:
                    wait(pe, bxt_copied, k - 2)
                    pe.wait_ge(ab_part3, k)
                pe.wait_ge(y_part3_ready, (k - 1) * GROUPS + g + 1)
                part1 = y_sb[(u - 1) % SLOTS][:, :].bitcast(BF16)
                part2 = y_rem[m][:, :].bitcast(BF16)
                for j in range(g * CPG, (g + 1) * CPG):
                    upper = slice(2 * P * j + 1, 2 * P * (j + 1), 2)
                    b_parts = ab_parts[m][:, j, KSLOTS:NPART, :]
                    for n, y_part in enumerate((part1[:, upper], part2[:, upper],
                                                y_part3[m][:, j * P:(j + 1) * P])):
                        mm = nc.tensor.matmul(bank[:, 0:BX_PARTS * R], y_part, b_parts,
                                              start=(j == 0 and n == 0),
                                              stop=(j == CHUNKS - 1 and n == 2))
                if g == GROUPS - 1:
                    mm.then_inc(bx_summed, 1)

            def turn_a(k, u, g):
                m = (u - 1) % 2
                if g == 0:
                    pe.wait_ge(a_slots_full, k)
                wait(pe, at_copied, (k - 1) * GROUPS + g - 1)
                for c in range(CPG):
                    mm = nc.tensor.transpose(at_ps[g % 2][:, c * P:(c + 1) * P],
                                             ab_parts[m][:, g * CPG + c, 0:KSLOTS, :].rearrange("p s r -> p (s r)"),
                                             ident_bf16[:, :])
                mm.then_inc(at_turned, 1)

            def turn_bx(k, u):
                pe.wait_ge(bx_split, (k - 1) * BX_OPS)
                nc.tensor.transpose(bx_ps[u % 2][:, 128:128 + P // 2].bitcast(BF16),
                                    bx_parts[:, :, :].rearrange("p s r -> p (s r)"),
                                    ident_bf16[:, :]).then_inc(bxt_turned, 1)

            def main(k, q, u, g):
                if g == 0:
                    pe.wait_ge(x_loaded[u], (q + 1) * 16)
                    pe.wait_ge(w_ready, k + 1)
                wait(pe, y_copied, k * GROUPS + g - 1)
                for c in range(CPG):
                    j = g * CPG + c
                    mm = nc.tensor.matmul(y_ps[g % 2][:, c * P:(c + 1) * P], x_sb[u][:, j * P:(j + 1) * P],
                                          w_sel[u % 2][:, :], start=True, stop=True)
                mm.then_inc(y_summed, 1)

            def update(k, u, g):
                if g == 0:
                    pe.wait_ge(bxt_copied, k - 1)
                pe.wait_ge(at_copied, (k - 2) * GROUPS + g + 1)
                wait(pe, z_ready, (k - 2) * GROUPS + g - 1)
                for c in range(CPG):
                    j = g * CPG + c
                    mm = nc.tensor.matmul(z_ps[g % 2][:, c * P:(c + 1) * P], at_sb[u % 2][:, j * P:(j + 1) * P],
                                          bxt_sb[u % 2][:, :], start=True, stop=True)
                mm.then_inc(z_summed, 1)

            def step(k, q, u):
                for g in range(GROUPS):
                    if live(k - 1):
                        project(k, u, g)
                        turn_a(k, u, g)
                    if live(k - 2) and g == 0:
                        turn_bx(k, u)
                    if live(k):
                        main(k, q, u, g)
                    if live(k - 2):
                        update(k, u, g)

            pe.wait_ge(ident_ready, 2)
            steps(pe, step, 1, BLOCKS, LAST)

        @block.scalar
        def _(act):
            def copy_at(k, u, g):
                if g == 0:
                    wait(act, z_summed, (k - 2) * GROUPS)
                act.wait_ge(at_turned, (k - 1) * GROUPS + g + 1)
                nc.scalar.activation(at_sb[(u - 1) % 2][:, g * GW:(g + 1) * GW], at_ps[g % 2][:, 0:GW],
                                     ACT.Copy).then_inc(at_copied, 1)

            def copy_bxt(k, u):
                wait(act, z_summed, (k - 3) * GROUPS)
                act.wait_ge(bxt_turned, k - 1)
                nc.scalar.activation(bxt_sb[u % 2][:, :], bx_ps[u % 2][:, 128:128 + P // 2].bitcast(BF16),
                                     ACT.Copy).then_inc(bxt_copied, 1)

            def copy_y(k, u, g):
                if g == 0:
                    wait(act, z_ready, (k - 3) * GROUPS)
                    wait(act, bx_summed, k - 3)
                act.wait_ge(y_summed, k * GROUPS + g + 1)
                nc.scalar.activation(y_sb[u][:, g * GW:(g + 1) * GW], y_ps[g % 2][:, :],
                                     ACT.Copy).then_inc(y_copied, 1)

            def cast(k, q, u, n, source, done):
                nc.scalar.activation(ab_parts[u % 2][:, :, n:NPART:KSLOTS, :].rearrange("p j m r -> p m j r"),
                                     source[:, :, :, :], ACT.Copy).then_inc(done, 1)

            def prepare(k, q, u, g):
                parts = ab_parts[u % 2]
                if g == 0:
                    act.wait_ge(ab_loaded[u], (q + 1) * 16)
                    wait(act, bx_summed, k - 1)
                    wait(act, at_turned, (k - 1) * GROUPS)
                    cast(k, q, u, 0, ab_sb[u], ab_part1)
                if g == 1:
                    act.wait_ge(ab_rem_ready, k + 1)
                    cast(k, q, u, 1, ab_rem, ab_part2)
                if g == 2:
                    act.wait_ge(ab_part3, k + 1)
                    act.wait_ge(ab_part2, k + 1)
                    nc.scalar.activation(parts[:, :, 3:6, :], parts[:, :, 0:3, :], ACT.Copy)
                    nc.scalar.activation(parts[:, :, 6:8, :], parts[:, :, 0:2, :], ACT.Copy).then_inc(a_slots_full, 1)

            def step(k, q, u):
                for g in range(GROUPS):
                    if live(k - 1):
                        copy_at(k, u, g)
                    if live(k - 2) and g == 0:
                        copy_bxt(k, u)
                    if live(k):
                        prepare(k, q, u, g)
                        copy_y(k, u, g)

            steps(act, step, 1, BLOCKS, LAST)

        @block.vector
        def _(dve):
            def split_bx(k, u):
                did = (k - 1) * BX_OPS
                dve.wait_ge(bx_summed, k)
                nc.vector.tensor_reduce(bx[:, :], bx_ps[(u - 1) % 2][:, 0:BX_PARTS * R].rearrange("p (m r) -> p r m", r=R),
                                        AX.X, ALU.add).then_inc(bx_split, 1)
                wait(dve, bxt_turned, k - 1)
                dve.wait_ge(bx_split, did + 1)
                nc.vector.tensor_copy(bx_parts[:, 0:3, :], bx[:, None, :].broadcast_to((P, 3, R))).then_inc(bx_split, 1)
                dve.wait_ge(bx_split, did + 2)
                nc.vector.tensor_tensor(bx_rem[:, :], bx[:, :], bx_parts[:, 0, :], ALU.subtract).then_inc(bx_split, 1)
                dve.wait_ge(bx_split, did + 3)
                nc.vector.tensor_copy(bx_parts[:, 3:6, :], bx_rem[:, None, :].broadcast_to((P, 3, R))).then_inc(bx_split, 1)
                dve.wait_ge(bx_split, did + 4)
                nc.vector.tensor_tensor(bx_parts[:, 6:8, :], bx_rem[:, None, :].broadcast_to((P, 2, R)),
                                        bx_parts[:, 3:5, :], ALU.subtract).then_inc(bx_split, 1)

            def y_remainder(k, u, g):
                if g == 0:
                    wait(dve, bx_summed, k - 1)
                    wait(dve, y_part3_ready, (k - 1) * GROUPS)
                dve.wait_ge(y_copied, k * GROUPS + g + 1)
                cols = slice(g * GW, (g + 1) * GW)
                upper = slice(2 * g * GW + 1, 2 * (g + 1) * GW, 2)
                nc.vector.tensor_tensor(y_rem[u % 2][:, cols], y_sb[u][:, cols], y_sb[u][:, :].bitcast(BF16)[:, upper],
                                        ALU.subtract).then_inc(y_rem_ready, 1)

            def prepare(k, u, g):
                parts = ab_parts[u % 2][:, :, :, :].rearrange("p j m r -> p m j r")
                if g == 0:
                    dve.wait_ge(ab_part1, k + 1)
                    wait(dve, ab_part3, k)
                    nc.vector.tensor_tensor(ab_rem[:, :, :, :], ab_sb[u][:, :, :, :], parts[:, 0:NPART:KSLOTS],
                                            ALU.subtract).then_inc(ab_rem_ready, 1)
                if g == 1:
                    dve.wait_ge(ab_part2, k + 1)
                    nc.vector.tensor_tensor(parts[:, 2:NPART:KSLOTS], ab_rem[:, :, :, :], parts[:, 1:NPART:KSLOTS],
                                            ALU.subtract).then_inc(ab_part3, 1)

            def add_z(k, q, u, g):
                s = (u - 2) % SLOTS
                if g == 0:
                    wait(dve, z_stored[s], turn(q, u, 2) * 16)
                dve.wait_ge(z_summed, (k - 2) * GROUPS + g + 1)
                cols = slice(g * GW, (g + 1) * GW)
                nc.vector.tensor_tensor(z_sb[s][:, cols], z_ps[g % 2][:, :], y_sb[s][:, cols],
                                        ALU.add).then_inc(z_ready, 1)

            def step(k, q, u):
                for g in range(GROUPS):
                    if live(k - 1) and g == GROUPS - 1:
                        split_bx(k, u)
                    if live(k):
                        y_remainder(k, u, g)
                        prepare(k, u, g)
                    if live(k - 2):
                        add_z(k, q, u, g)

            steps(dve, step, 2, BLOCKS, LAST)

        @block.gpsimd
        def _(pool):
            nc.gpsimd.memset(ident_f32[:, :], 0.0).then_inc(zeroed, 1)
            nc.gpsimd.memset(ident_bf16[:, :], 0.0).then_inc(zeroed, 1)
            pool.wait_ge(zeroed, 2)
            for ident in (ident_f32, ident_bf16):
                nc.gpsimd.affine_select(out=ident[:, :], in_=ident[:, :], compare_op=ALU.not_equal, fill=1.0, base=0,
                                        pattern=[[-1, P]], channel_multiplier=1).then_inc(ident_ready, 1)
            pool.wait_ge(ident_ready, 2)
            pool.wait_ge(ids_loaded, 32)
            pool.wait_ge(tables_loaded, 16)

            def select_w(b, m):
                e = pool.value_load(ids_cond[0:1, bass.ds(b, 1)], min_val=0, max_val=EXPERTS - 1)
                nc.gpsimd.tensor_tensor(w_sel[m][:, :], w_table[:, bass.ds(e * C, C)], ident_f32[:, :],
                                        ALU.add).then_inc(w_ready, 1)

            def step(k, q, u):
                for g in range(GROUPS):
                    pool.wait_ge(y_rem_ready, k * GROUPS + g + 1)
                    if g == 0:
                        wait(pool, bx_summed, k - 1)
                        if not isinstance(k, int) or live(k + 1):
                            wait(pool, y_summed, k * GROUPS)
                            select_w(k + 1, (u + 1) % 2)
                    cols = slice(g * GW, (g + 1) * GW)
                    upper = slice(2 * g * GW + 1, 2 * (g + 1) * GW, 2)
                    nc.gpsimd.tensor_tensor(y_part3[u % 2][:, cols], y_rem[u % 2][:, cols],
                                            y_rem[u % 2][:, :].bitcast(BF16)[:, upper],
                                            ALU.subtract).then_inc(y_part3_ready, 1)

            select_w(0, 0)
            steps(pool, step, 1, BLOCKS - 1, BATCHES - 1)


def kernel(x, itok_B_0_15, itok_B_4_50, L0_cond_weights, L1_cond_A, L1_cond_B):
    import numpy as np
    import concourse.bacc as bacc
    from concourse.bass_utils import run_bass_kernel_spmd

    x, w = np.asarray(x), np.asarray(L0_cond_weights)
    a, b = np.asarray(L1_cond_A), np.asarray(L1_cond_B)
    batches, c, t = x.shape
    adapters, rank = b.shape[:2]
    chunks = t // P
    a_laid = a.reshape(adapters, chunks, P, rank).transpose(0, 2, 1, 3)
    b_laid = b.reshape(adapters, rank, chunks, P).transpose(0, 3, 2, 1)
    arrays = {
        "x_dram": np.ascontiguousarray(x),
        "cond_dram": np.ascontiguousarray(itok_B_0_15).reshape(1, batches),
        "adapter_dram": np.ascontiguousarray(itok_B_4_50).reshape(1, batches),
        "w_dram": np.ascontiguousarray(w.transpose(1, 0, 2)),
        "ab_dram": np.ascontiguousarray(np.stack([a_laid, b_laid], axis=2)).reshape(adapters, P, -1),
    }
    nc = bacc.Bacc("TRN2", target_bir_lowering=False, num_devices=1)
    ins = [nc.dram_tensor(n, v.shape, mybir.dt.from_np(v.dtype), kind="ExternalInput").ap()
           for n, v in arrays.items()]
    out = nc.dram_tensor("z_dram", (batches, P, t), F32, kind="ExternalOutput").ap()
    build(nc, *ins, out)
    got = run_bass_kernel_spmd(nc, [arrays], core_ids=[0]).results[0]["z_dram"]
    return np.ascontiguousarray(got.reshape(batches, P, chunks, c).transpose(0, 3, 2, 1)).reshape(x.shape)
```

```python
from contextlib import ExitStack

import concourse.bass as bass
from concourse import mybir

F32 = mybir.dt.float32
BF16 = mybir.dt.bfloat16
I32 = mybir.dt.int32
ALU = mybir.AluOpType
ACT = mybir.ActivationFunctionType
AX = mybir.AxisListType

P = 128
GROUPS = 4
SLOTS = 4
BX_PARTS = 3
UPDATE_LAG = 3
KSLOTS = 8
NPART = KSLOTS + BX_PARTS


def build(nc, x, cond, adapter, w, ab, out):
    BATCHES, C, T = x.shape
    EXPERTS = w.shape[1]
    ADAPTERS = ab.shape[0]
    CHUNKS = T // P
    R = ab.shape[2] // (2 * CHUNKS)
    CPG = CHUNKS // GROUPS
    GW = CPG * P
    BLOCKS = BATCHES // SLOTS
    assert C == P and KSLOTS * R == P and GW * 4 == 2048 and BATCHES % SLOTS == 0

    with ExitStack() as ctx:
        def sb(name, shape, dt):
            return ctx.enter_context(nc.sbuf_tensor(name, shape, dt))

        def psum(name, shape, dt):
            return ctx.enter_context(nc.psum_tensor(name, shape, dt))

        def sem(name):
            return ctx.enter_context(nc.semaphore(name))

        ids_cond = sb("ids_cond", [1, BATCHES], I32)
        ids_adapter = sb("ids_adapter", [1, BATCHES], I32)
        w_table = sb("w_table", [P, EXPERTS * C], F32)
        ident_f32 = sb("ident_f32", [P, P], F32)
        ident_bf16 = sb("ident_bf16", [P, P], BF16)
        x_sb = [sb(f"x_sb{s}", [P, T], F32) for s in range(SLOTS)]
        ab_sb = [sb(f"ab_sb{s}", [P, 2, CHUNKS, R], F32) for s in range(SLOTS)]
        y_sb = [sb(f"y_sb{s}", [P, T], F32) for s in range(SLOTS)]
        z_sb = [sb(f"z_sb{s}", [P, T], F32) for s in range(SLOTS)]
        w_sel = [sb(f"w_sel{s}", [P, C], F32) for s in range(2)]
        y_rem = [sb(f"y_rem{s}", [P, T], F32) for s in range(2)]
        y_part3 = [sb(f"y_part3{s}", [P, T], BF16) for s in range(2)]
        ab_parts = [sb(f"ab_parts{s}", [P, CHUNKS, NPART, R], BF16) for s in range(SLOTS)]
        ab_rem = sb("ab_rem", [P, 2, CHUNKS, R], F32)
        at_sb = [sb(f"at_sb{s}", [P, T], BF16) for s in range(2)]
        bx = sb("bx", [P, R], F32)
        bx_rem = sb("bx_rem", [P, R], F32)
        bx_parts = sb("bx_parts", [P, KSLOTS, R], BF16)
        bxt_sb = [sb(f"bxt_sb{s}", [P, P], BF16) for s in range(2)]

        y_ps = [psum(f"y_ps{s}", [P, GW], F32) for s in range(2)]
        z_ps = [psum(f"z_ps{s}", [P, GW], F32) for s in range(2)]
        at_ps = [psum(f"at_ps{s}", [P, 2 * GW], BF16) for s in range(2)]
        bx_ps = [psum(f"bx_ps{s}", [P, 512], F32) for s in range(2)]

        tables_loaded = sem("tables_loaded")
        ids_loaded = sem("ids_loaded")
        x_loaded = [sem(f"x_loaded{s}") for s in range(SLOTS)]
        ab_loaded = [sem(f"ab_loaded{s}") for s in range(SLOTS)]
        z_stored = [sem(f"z_stored{s}") for s in range(SLOTS)]
        zeroed = sem("zeroed")
        ident_ready = sem("ident_ready")
        w_ready = sem("w_ready")
        y_summed = sem("y_summed")
        y_copied = sem("y_copied")
        y_rem_ready = sem("y_rem_ready")
        y_part3_ready = sem("y_part3_ready")
        ab_part1 = sem("ab_part1")
        ab_rem_ready = sem("ab_rem_ready")
        ab_part2 = sem("ab_part2")
        ab_part3 = sem("ab_part3")
        a_slots_full = sem("a_slots_full")
        at_turned = sem("at_turned")
        at_copied = sem("at_copied")
        bx_summed = sem("bx_summed")
        bx_split = sem("bx_split")
        bxt_turned = sem("bxt_turned")
        bxt_copied = sem("bxt_copied")
        z_summed = sem("z_summed")
        z_ready = sem("z_ready")
        BX_OPS = 5

        def live(k):
            return not isinstance(k, int) or 0 <= k < BATCHES

        def wait(eng, semaphore, value):
            if not isinstance(value, int) or value > 0:
                eng.wait_ge(semaphore, value)

        def turn(q, u, lag):
            return q - 1 if u < lag else q

        def lagged(k, q, u, g, lag):
            if g >= lag:
                return k, q, u, g - lag
            return k - 1, turn(q, u, 1), (u - 1) % SLOTS, g - lag + GROUPS

        def steps(eng, step, first_block, end_block, last):
            for k in range(SLOTS * first_block):
                step(k, k // SLOTS, k % SLOTS)
            with eng.Fori(first_block, end_block) as q:
                for u in range(SLOTS):
                    step(q * SLOTS + u, q, u)
            for k in range(SLOTS * end_block, last + 1):
                step(k, k // SLOTS, k % SLOTS)

        LAST = BATCHES + 2

        block = ctx.enter_context(nc.Block())

        @block.sync
        def _(sp):
            def load(b, s):
                sp.dma_start(x_sb[s][:, :], x[bass.ds(b, 1)].rearrange("o c t -> (o c) t")).then_inc(x_loaded[s], 16)
                a = sp.value_load(ids_adapter[0:1, bass.ds(b, 1)], min_val=0, max_val=ADAPTERS - 1)
                sp.dma_start(ab_sb[s][:, :, :, :].rearrange("p m j r -> p (m j r)"),
                             ab[bass.ds(a, 1)].rearrange("o p f -> (o p) f")).then_inc(ab_loaded[s], 16)

            sp.dma_start(ids_adapter[:, :], adapter).then_inc(ids_loaded, 16)
            sp.dma_start(ids_cond[:, :], cond).then_inc(ids_loaded, 16)
            sp.dma_start(w_table[:, :], w.rearrange("c e d -> c (e d)")).then_inc(tables_loaded, 16)
            sp.wait_ge(ids_loaded, 32)
            for b in range(SLOTS):
                load(b, b)

            def step(k, q, u):
                if live(k - 3):
                    s = (u - 3) % SLOTS
                    sp.wait_ge(z_ready, (k - 2) * GROUPS)
                    sp.dma_start(out[bass.ds(k - 3, 1)].rearrange("o p f -> (o p) f"),
                                 z_sb[s][:, :]).then_inc(z_stored[s], 16)
                if live(k) and (not isinstance(k, int) or live(k + SLOTS)):
                    sp.wait_ge(y_summed, (k + 1) * GROUPS)
                    sp.wait_ge(ab_rem_ready, k + 1)
                    sp.wait_ge(ab_part1, k + 1)
                    load(k + SLOTS, u)

            steps(sp, step, 1, BLOCKS - 1, LAST)
            for s in range(SLOTS):
                sp.wait_ge(z_stored[s], 16 * BLOCKS)

        @block.tensor
        def _(pe):
            def project(k, u, g):
                bank, m = bx_ps[(u - 1) % 2], (u - 1) % 2
                if g == 0:
                    wait(pe, bxt_copied, k - 2)
                    pe.wait_ge(ab_part3, k)
                pe.wait_ge(y_part3_ready, (k - 1) * GROUPS + g + 1)
                part1 = y_sb[(u - 1) % SLOTS][:, :].bitcast(BF16)
                part2 = y_rem[m][:, :].bitcast(BF16)
                for j in range(g * CPG, (g + 1) * CPG):
                    upper = slice(2 * P * j + 1, 2 * P * (j + 1), 2)
                    b_parts = ab_parts[(u - 1) % SLOTS][:, j, KSLOTS:NPART, :]
                    for n, y_part in enumerate((part1[:, upper], part2[:, upper],
                                                y_part3[m][:, j * P:(j + 1) * P])):
                        mm = nc.tensor.matmul(bank[:, 0:BX_PARTS * R], y_part, b_parts,
                                              start=(j == 0 and n == 0),
                                              stop=(j == CHUNKS - 1 and n == 2))
                if g == GROUPS - 1:
                    mm.then_inc(bx_summed, 1)

            def turn_a(k, u, g):
                parts = ab_parts[(u - 1) % SLOTS]
                if g == 0:
                    pe.wait_ge(a_slots_full, k)
                wait(pe, at_copied, (k - 1) * GROUPS + g - 1)
                for c in range(CPG):
                    mm = nc.tensor.transpose(at_ps[g % 2][:, c * P:(c + 1) * P],
                                             parts[:, g * CPG + c, 0:KSLOTS, :].rearrange("p s r -> p (s r)"),
                                             ident_bf16[:, :])
                mm.then_inc(at_turned, 1)

            def turn_bx(k, u):
                pe.wait_ge(bx_split, (k - 1) * BX_OPS)
                nc.tensor.transpose(bx_ps[u % 2][:, 128:128 + P // 2].bitcast(BF16),
                                    bx_parts[:, :, :].rearrange("p s r -> p (s r)"),
                                    ident_bf16[:, :]).then_inc(bxt_turned, 1)

            def main(k, q, u, g):
                if g == 0:
                    pe.wait_ge(x_loaded[u], (q + 1) * 16)
                    pe.wait_ge(w_ready, k + 1)
                wait(pe, y_copied, k * GROUPS + g - 1)
                for c in range(CPG):
                    j = g * CPG + c
                    mm = nc.tensor.matmul(y_ps[g % 2][:, c * P:(c + 1) * P], x_sb[u][:, j * P:(j + 1) * P],
                                          w_sel[u % 2][:, :], start=True, stop=True)
                mm.then_inc(y_summed, 1)

            def update(k, u, g):
                if g == 0:
                    pe.wait_ge(bxt_copied, k - 1)
                pe.wait_ge(at_copied, (k - 2) * GROUPS + g + 1)
                wait(pe, z_ready, (k - 2) * GROUPS + g - 1)
                for c in range(CPG):
                    j = g * CPG + c
                    mm = nc.tensor.matmul(z_ps[g % 2][:, c * P:(c + 1) * P], at_sb[u % 2][:, j * P:(j + 1) * P],
                                          bxt_sb[u % 2][:, :], start=True, stop=True)
                mm.then_inc(z_summed, 1)

            def step(k, q, u):
                for g in range(GROUPS):
                    if live(k - 1):
                        project(k, u, g)
                        turn_a(k, u, g)
                    if live(k):
                        main(k, q, u, g)
                    if live(k - 2) and g == 2:
                        turn_bx(k, u)
                    k2, _, u2, g2 = lagged(k, q, u, g, UPDATE_LAG)
                    if live(k2 - 2):
                        update(k2, u2, g2)

            pe.wait_ge(ident_ready, 2)
            steps(pe, step, 1, BLOCKS, LAST)

        @block.scalar
        def _(act):
            def copy_at(k, u, g):
                wait(act, z_summed, (k - 3) * GROUPS + g + 1)
                act.wait_ge(at_turned, (k - 1) * GROUPS + g + 1)
                nc.scalar.activation(at_sb[(u - 1) % 2][:, g * GW:(g + 1) * GW], at_ps[g % 2][:, 0:GW],
                                     ACT.Copy).then_inc(at_copied, 1)

            def copy_bxt(k, u):
                wait(act, z_summed, (k - 3) * GROUPS)
                act.wait_ge(bxt_turned, k - 1)
                nc.scalar.activation(bxt_sb[u % 2][:, :], bx_ps[u % 2][:, 128:128 + P // 2].bitcast(BF16),
                                     ACT.Copy).then_inc(bxt_copied, 1)

            def copy_y(k, u, g):
                if g == 0:
                    wait(act, z_ready, (k - 3) * GROUPS)
                    wait(act, bx_summed, k - 3)
                act.wait_ge(y_summed, k * GROUPS + g + 1)
                nc.scalar.activation(y_sb[u][:, g * GW:(g + 1) * GW], y_ps[g % 2][:, :],
                                     ACT.Copy).then_inc(y_copied, 1)

            def cast(s, n, source, done):
                nc.scalar.activation(ab_parts[s][:, :, n:NPART:KSLOTS, :].rearrange("p j m r -> p m j r"),
                                     source[:, :, :, :], ACT.Copy).then_inc(done, 1)

            def round_ab(b, q, s, part):
                if part == 1:
                    act.wait_ge(ab_loaded[s], (q + 1) * 16)
                    wait(act, bx_summed, b - 3)
                    wait(act, at_turned, (b - 3) * GROUPS)
                    cast(s, 0, ab_sb[s], ab_part1)
                else:
                    act.wait_ge(ab_rem_ready, b + 1)
                    cast(s, 1, ab_rem, ab_part2)

            def repeat_a(k, u, g):
                parts = ab_parts[u]
                if g == 2:
                    act.wait_ge(ab_part3, k + 1)
                    act.wait_ge(ab_part2, k + 1)
                    nc.scalar.activation(parts[:, :, 3:6, :], parts[:, :, 0:3, :], ACT.Copy)
                if g == 3:
                    nc.scalar.activation(parts[:, :, 6:8, :], parts[:, :, 0:2, :], ACT.Copy).then_inc(a_slots_full, 1)

            def step(k, q, u):
                for g in range(GROUPS):
                    if live(k - 1):
                        copy_at(k, u, g)
                    if live(k + 1) and g in (0, 3):
                        round_ab(k + 1, q + (u + 1) // SLOTS, (u + 1) % SLOTS, 1 if g == 0 else 2)

                    if live(k):
                        copy_y(k, u, g)
                    if live(k - 2) and g == 2:
                        copy_bxt(k, u)
                    if live(k) and g in (1, 2):
                        repeat_a(k, u, g + 1)

            round_ab(0, 0, 0, 1)
            round_ab(0, 0, 0, 2)
            steps(act, step, 1, BLOCKS - 1, LAST)

        @block.vector
        def _(dve):
            def split_bx(k, u, op):
                done = (k - 1) * BX_OPS + op
                if op == 0:
                    dve.wait_ge(bx_summed, k)
                    ins = nc.vector.tensor_reduce(
                        bx[:, :], bx_ps[(u - 1) % 2][:, 0:BX_PARTS * R].rearrange("p (m r) -> p r m", r=R),
                        AX.X, ALU.add)
                else:
                    dve.wait_ge(bx_split, done)
                if op == 1:
                    wait(dve, bxt_turned, k - 1)
                    ins = nc.vector.tensor_copy(bx_parts[:, 0:3, :], bx[:, None, :].broadcast_to((P, 3, R)))
                if op == 2:
                    ins = nc.vector.tensor_tensor(bx_rem[:, :], bx[:, :], bx_parts[:, 0, :], ALU.subtract)
                if op == 3:
                    ins = nc.vector.tensor_copy(bx_parts[:, 3:6, :], bx_rem[:, None, :].broadcast_to((P, 3, R)))
                if op == 4:
                    ins = nc.vector.tensor_tensor(bx_parts[:, 6:8, :], bx_rem[:, None, :].broadcast_to((P, 2, R)),
                                                  bx_parts[:, 3:5, :], ALU.subtract)
                ins.then_inc(bx_split, 1)

            def y_remainder(k, u, g):
                if g == 0:
                    wait(dve, bx_summed, k - 1)
                    wait(dve, y_part3_ready, (k - 1) * GROUPS)
                dve.wait_ge(y_copied, k * GROUPS + g + 1)
                cols = slice(g * GW, (g + 1) * GW)
                upper = slice(2 * g * GW + 1, 2 * (g + 1) * GW, 2)
                nc.vector.tensor_tensor(y_rem[u % 2][:, cols], y_sb[u][:, cols], y_sb[u][:, :].bitcast(BF16)[:, upper],
                                        ALU.subtract).then_inc(y_rem_ready, 1)

            def part3_ab(k, u):
                dve.wait_ge(ab_part2, k + 1)
                parts = ab_parts[u][:, :, :, :].rearrange("p j m r -> p m j r")
                nc.vector.tensor_tensor(parts[:, 2:NPART:KSLOTS], ab_rem[:, :, :, :], parts[:, 1:NPART:KSLOTS],
                                        ALU.subtract).then_inc(ab_part3, 1)

            def add_z(k, q, u, g):
                s = (u - 2) % SLOTS
                if g == 0:
                    wait(dve, z_stored[s], turn(q, u, 2) * 16)
                dve.wait_ge(z_summed, (k - 2) * GROUPS + g + 1)
                cols = slice(g * GW, (g + 1) * GW)
                nc.vector.tensor_tensor(z_sb[s][:, cols], z_ps[g % 2][:, :], y_sb[s][:, cols],
                                        ALU.add).then_inc(z_ready, 1)

            def step(k, q, u):
                for g in range(GROUPS):
                    k2, q2, u2, g2 = lagged(k, q, u, g, UPDATE_LAG + 1)
                    if live(k2 - 2):
                        add_z(k2, q2, u2, g2)
                    if live(k - 1) and g == GROUPS - 1:
                        split_bx(k, u, 0)
                    if live(k - 2) and g < 2:
                        split_bx(k - 1, (u - 1) % SLOTS, 2 if g == 0 else 4)
                    if live(k):
                        y_remainder(k, u, g)
                    if live(k - 1) and g == GROUPS - 1:
                        split_bx(k, u, 1)
                    if live(k - 2) and g == 0:
                        split_bx(k - 1, (u - 1) % SLOTS, 3)
                    if live(k) and g == 0:
                        part3_ab(k, u)

            steps(dve, step, 2, BLOCKS, LAST)

        @block.gpsimd
        def _(pool):
            nc.gpsimd.memset(ident_f32[:, :], 0.0).then_inc(zeroed, 1)
            nc.gpsimd.memset(ident_bf16[:, :], 0.0).then_inc(zeroed, 1)
            pool.wait_ge(zeroed, 2)
            for ident in (ident_f32, ident_bf16):
                nc.gpsimd.affine_select(out=ident[:, :], in_=ident[:, :], compare_op=ALU.not_equal, fill=1.0, base=0,
                                        pattern=[[-1, P]], channel_multiplier=1).then_inc(ident_ready, 1)
            pool.wait_ge(ident_ready, 2)
            pool.wait_ge(ids_loaded, 32)
            pool.wait_ge(tables_loaded, 16)

            def select_w(b, m):
                e = pool.value_load(ids_cond[0:1, bass.ds(b, 1)], min_val=0, max_val=EXPERTS - 1)
                nc.gpsimd.tensor_tensor(w_sel[m][:, :], w_table[:, bass.ds(e * C, C)], ident_f32[:, :],
                                        ALU.add).then_inc(w_ready, 1)

            def remainder_ab(b, s):
                pool.wait_ge(ab_part1, b + 1)
                wait(pool, ab_part3, b)
                wait(pool, ab_part2, b)
                nc.gpsimd.tensor_tensor(ab_rem[:, :, :, :], ab_sb[s][:, :, :, :],
                                        ab_parts[s][:, :, 0:NPART:KSLOTS, :].rearrange("p j m r -> p m j r"),
                                        ALU.subtract).then_inc(ab_rem_ready, 1)

            def step(k, q, u):
                for g in range(GROUPS):
                    if g == 1 and (not isinstance(k, int) or live(k + 1)):
                        remainder_ab(k + 1, (u + 1) % SLOTS)
                    pool.wait_ge(y_rem_ready, k * GROUPS + g + 1)
                    if g == 0:
                        wait(pool, bx_summed, k - 1)
                        if not isinstance(k, int) or live(k + 1):
                            wait(pool, y_summed, k * GROUPS)
                            select_w(k + 1, (u + 1) % 2)
                    cols = slice(g * GW, (g + 1) * GW)
                    upper = slice(2 * g * GW + 1, 2 * (g + 1) * GW, 2)
                    nc.gpsimd.tensor_tensor(y_part3[u % 2][:, cols], y_rem[u % 2][:, cols],
                                            y_rem[u % 2][:, :].bitcast(BF16)[:, upper],
                                            ALU.subtract).then_inc(y_part3_ready, 1)

            remainder_ab(0, 0)
            select_w(0, 0)
            steps(pool, step, 1, BLOCKS - 1, BATCHES - 1)


def kernel(x, itok_B_0_15, itok_B_4_50, L0_cond_weights, L1_cond_A, L1_cond_B):
    import numpy as np
    import concourse.bacc as bacc
    from concourse.bass_utils import run_bass_kernel_spmd

    x, w = np.asarray(x), np.asarray(L0_cond_weights)
    a, b = np.asarray(L1_cond_A), np.asarray(L1_cond_B)
    batches, c, t = x.shape
    adapters, rank = b.shape[:2]
    chunks = t // P
    a_laid = a.reshape(adapters, chunks, P, rank).transpose(0, 2, 1, 3)
    b_laid = b.reshape(adapters, rank, chunks, P).transpose(0, 3, 2, 1)
    arrays = {
        "x_dram": np.ascontiguousarray(x),
        "cond_dram": np.ascontiguousarray(itok_B_0_15).reshape(1, batches),
        "adapter_dram": np.ascontiguousarray(itok_B_4_50).reshape(1, batches),
        "w_dram": np.ascontiguousarray(w.transpose(1, 0, 2)),
        "ab_dram": np.ascontiguousarray(np.stack([a_laid, b_laid], axis=2)).reshape(adapters, P, -1),
    }
    nc = bacc.Bacc("TRN2", target_bir_lowering=False, num_devices=1)
    ins = [nc.dram_tensor(n, v.shape, mybir.dt.from_np(v.dtype), kind="ExternalInput").ap()
           for n, v in arrays.items()]
    out = nc.dram_tensor("z_dram", (batches, P, t), F32, kind="ExternalOutput").ap()
    build(nc, *ins, out)
    got = run_bass_kernel_spmd(nc, [arrays], core_ids=[0]).results[0]["z_dram"]
    return np.ascontiguousarray(got.reshape(batches, P, chunks, c).transpose(0, 3, 2, 1)).reshape(x.shape)
```

```python
from contextlib import ExitStack

import concourse.bass as bass
from concourse import mybir

F32 = mybir.dt.float32
BF16 = mybir.dt.bfloat16
I32 = mybir.dt.int32
ALU = mybir.AluOpType
ACT = mybir.ActivationFunctionType
AX = mybir.AxisListType

P = 128
GROUPS = 4
SLOTS = 4
BODY = 2
BX_PARTS = 3
UPDATE_LAG = 3
KSLOTS = 8
NPART = KSLOTS + BX_PARTS


def build(nc, x, cond, adapter, w, ab, out):
    BATCHES, C, T = x.shape
    EXPERTS = w.shape[1]
    ADAPTERS = ab.shape[0]
    CHUNKS = T // P
    R = ab.shape[2] // (2 * CHUNKS)
    CPG = CHUNKS // GROUPS
    GW = CPG * P
    BLOCKS = BATCHES // SLOTS
    assert C == P and KSLOTS * R == P and GW * 4 == 2048 and BATCHES % SLOTS == 0

    with ExitStack() as ctx:
        def sb(name, shape, dt):
            return ctx.enter_context(nc.sbuf_tensor(name, shape, dt))

        def psum(name, shape, dt):
            return ctx.enter_context(nc.psum_tensor(name, shape, dt))

        def sem(name):
            return ctx.enter_context(nc.semaphore(name))

        ids_cond = sb("ids_cond", [1, BATCHES], I32)
        ids_adapter = sb("ids_adapter", [1, BATCHES], I32)
        w_first = sb("w_first", [P, SLOTS * C], F32)
        w_table = sb("w_table", [P, EXPERTS * C], F32)
        ident_f32 = sb("ident_f32", [P, P], F32)
        ident_bf16 = sb("ident_bf16", [P, P], BF16)
        x_sb = [sb(f"x_sb{s}", [P, T], F32) for s in range(SLOTS)]
        ab_sb = [sb(f"ab_sb{s}", [P, 2, CHUNKS, R], F32) for s in range(SLOTS)]
        y_sb = [sb(f"y_sb{s}", [P, T], F32) for s in range(SLOTS)]
        z_sb = [sb(f"z_sb{s}", [P, T], F32) for s in range(SLOTS)]
        w_sel = [sb(f"w_sel{s}", [P, C], F32) for s in range(2)]
        y_rem = [sb(f"y_rem{s}", [P, T], F32) for s in range(2)]
        y_part3 = [sb(f"y_part3{s}", [P, T], BF16) for s in range(2)]
        ab_parts = [sb(f"ab_parts{s}", [P, CHUNKS, NPART, R], BF16) for s in range(SLOTS)]
        ab_rem = sb("ab_rem", [P, 2, CHUNKS, R], F32)
        at_sb = [sb(f"at_sb{s}", [P, T], BF16) for s in range(2)]
        bx = sb("bx", [P, R], F32)
        bx_rem = sb("bx_rem", [P, R], F32)
        bx_parts = sb("bx_parts", [P, KSLOTS, R], BF16)
        bxt_sb = [sb(f"bxt_sb{s}", [P, P], BF16) for s in range(2)]

        y_ps = [psum(f"y_ps{s}", [P, GW], F32) for s in range(2)]
        z_ps = [psum(f"z_ps{s}", [P, GW], F32) for s in range(2)]
        at_ps = [psum(f"at_ps{s}", [P, 2 * GW], BF16) for s in range(2)]
        bx_ps = [psum(f"bx_ps{s}", [P, 512], F32) for s in range(2)]

        w_first_loaded = [sem(f"w_first_loaded{s}") for s in range(SLOTS)]
        w_table_loaded = sem("w_table_loaded")
        cond_loaded = sem("cond_loaded")
        adapter_loaded = sem("adapter_loaded")
        x_first_half = sem("x_first_half")
        x_loaded = [sem(f"x_loaded{s}") for s in range(SLOTS)]
        ab_loaded = [sem(f"ab_loaded{s}") for s in range(SLOTS)]
        z_stored = [sem(f"z_stored{s}") for s in range(SLOTS)]
        zeroed = sem("zeroed")
        ident_ready = sem("ident_ready")
        w_ready = sem("w_ready")
        y_summed = sem("y_summed")
        y_copied = sem("y_copied")
        y_rem_ready = sem("y_rem_ready")
        y_part3_ready = sem("y_part3_ready")
        ab_part1 = sem("ab_part1")
        ab_rem_ready = sem("ab_rem_ready")
        ab_part2 = sem("ab_part2")
        a_part3 = sem("a_part3")
        b_part3 = sem("b_part3")
        a_slots_full = sem("a_slots_full")
        at_turned = sem("at_turned")
        at_copied = sem("at_copied")
        bx_summed = sem("bx_summed")
        bx_split = sem("bx_split")
        bxt_turned = sem("bxt_turned")
        bxt_copied = sem("bxt_copied")
        z_summed = sem("z_summed")
        z_ready = sem("z_ready")
        BX_OPS = 5

        def live(k):
            return not isinstance(k, int) or 0 <= k < BATCHES

        def wait(eng, semaphore, value):
            if not isinstance(value, int) or value > 0:
                eng.wait_ge(semaphore, value)

        def turn(q, u, lag):
            return q - 1 if u < lag else q

        def lagged(k, q, u, g, lag):
            if g >= lag:
                return k, q, u, g - lag
            return k - 1, turn(q, u, 1), (u - 1) % SLOTS, g - lag + GROUPS

        def steps(eng, step, first_block, end_block, last):
            for k in range(SLOTS * first_block):
                step(k, k // SLOTS, k % SLOTS)
            assert (end_block - first_block) % BODY == 0
            with nc.Fori(0, (end_block - first_block) // BODY, engines=(eng.engine,), hint_back_edge=True) as i:
                for n in range(BODY):
                    q = i * BODY + (first_block + n)
                    for u in range(SLOTS):
                        step(q * SLOTS + u, q, u)
            for k in range(SLOTS * end_block, last + 1):
                step(k, k // SLOTS, k % SLOTS)

        LAST = BATCHES + 2

        block = ctx.enter_context(nc.Block())

        @block.sync
        def _(sp):
            def load_x(b, s):
                sp.dma_start(x_sb[s][:, :], x[bass.ds(b, 1)].rearrange("o c t -> (o c) t")).then_inc(x_loaded[s], 16)

            def load_ab(b, s):
                a = sp.value_load(ids_adapter[0:1, bass.ds(b, 1)], min_val=0, max_val=ADAPTERS - 1)
                sp.dma_start(ab_sb[s][:, :, :, :].rearrange("p m j r -> p (m j r)"),
                             ab[bass.ds(a, 1)].rearrange("o p f -> (o p) f")).then_inc(ab_loaded[s], 16)

            def load_w_first(b):
                e = sp.value_load(ids_cond[0:1, b:b + 1], min_val=0, max_val=EXPERTS - 1)
                sp.dma_start(w_first[:, b * C:(b + 1) * C],
                             w[:, bass.ds(e, 1)].rearrange("c o d -> c (o d)")).then_inc(w_first_loaded[b], 16)

            half = T // 2
            sp.dma_start(ids_cond[:, :], cond).then_inc(cond_loaded, 16)
            sp.dma_start(ids_adapter[:, :], adapter).then_inc(adapter_loaded, 16)
            sp.dma_start(x_sb[0][:, 0:half], x[0, :, 0:half]).then_inc(x_first_half, 16)
            sp.wait_ge(cond_loaded, 16)
            load_w_first(0)
            sp.wait_ge(adapter_loaded, 16)
            load_ab(0, 0)
            sp.dma_start(x_sb[0][:, half:T], x[0, :, half:T]).then_inc(x_loaded[0], 16)
            for b in range(1, SLOTS):
                load_ab(b, b)
                load_w_first(b)
                load_x(b, b)
            sp.dma_start(w_table[:, :], w.rearrange("c e d -> c (e d)")).then_inc(w_table_loaded, 16)

            def step(k, q, u):
                if live(k - 3):
                    s = (u - 3) % SLOTS
                    pieces = GROUPS if isinstance(k, int) and k - 3 >= BATCHES - SLOTS else 1
                    for i in range(pieces):
                        cols = slice(i * T // pieces, (i + 1) * T // pieces)
                        sp.wait_ge(z_ready, (k - 3) * GROUPS + (i + 1) * GROUPS // pieces)
                        sp.dma_start(out[bass.ds(k - 3, 1), :, cols].rearrange("o p f -> (o p) f"),
                                     z_sb[s][:, cols]).then_inc(z_stored[s], 16)
                if live(k) and (not isinstance(k, int) or live(k + SLOTS)):
                    sp.wait_ge(y_summed, (k + 1) * GROUPS)
                    sp.wait_ge(ab_rem_ready, k + 1)
                    sp.wait_ge(ab_part1, k + 1)
                    load_x(k + SLOTS, u)
                    load_ab(k + SLOTS, u)

            steps(sp, step, 1, BLOCKS - 1, LAST)
            for s in range(SLOTS):
                sp.wait_ge(z_stored[s], 16 * (BLOCKS - 1 + GROUPS))

        @block.tensor
        def _(pe):
            def project(k, u, g):
                bank, m = bx_ps[(u - 1) % 2], (u - 1) % 2
                if g == 0:
                    wait(pe, bxt_copied, k - 2)
                    pe.wait_ge(b_part3, k)
                pe.wait_ge(y_part3_ready, (k - 1) * GROUPS + g + 1)
                part1 = y_sb[(u - 1) % SLOTS][:, :].bitcast(BF16)
                part2 = y_rem[m][:, :].bitcast(BF16)
                for j in range(g * CPG, (g + 1) * CPG):
                    upper = slice(2 * P * j + 1, 2 * P * (j + 1), 2)
                    b_parts = ab_parts[(u - 1) % SLOTS][:, j, KSLOTS:NPART, :]
                    for n, y_part in enumerate((part1[:, upper], part2[:, upper],
                                                y_part3[m][:, j * P:(j + 1) * P])):
                        mm = nc.tensor.matmul(bank[:, 0:BX_PARTS * R], y_part, b_parts,
                                              start=(j == 0 and n == 0),
                                              stop=(j == CHUNKS - 1 and n == 2))
                if g == GROUPS - 1:
                    mm.then_inc(bx_summed, 1)

            def turn_a(k, u, g):
                parts = ab_parts[(u - 1) % SLOTS]
                if g == 0:
                    pe.wait_ge(a_slots_full, k)
                wait(pe, at_copied, (k - 1) * GROUPS + g - 1)
                for c in range(CPG):
                    mm = nc.tensor.transpose(at_ps[g % 2][:, c * P:(c + 1) * P],
                                             parts[:, g * CPG + c, 0:KSLOTS, :].rearrange("p s r -> p (s r)"),
                                             ident_bf16[:, :])
                mm.then_inc(at_turned, 1)

            def turn_bx(k, u):
                pe.wait_ge(bx_split, (k - 1) * BX_OPS)
                nc.tensor.transpose(bx_ps[u % 2][:, 128:128 + P // 2].bitcast(BF16),
                                    bx_parts[:, :, :].rearrange("p s r -> p (s r)"),
                                    ident_bf16[:, :]).then_inc(bxt_turned, 1)

            def main(k, q, u, g):
                if g == 0:
                    pe.wait_ge(w_ready, k + 1)
                if isinstance(k, int) and k == 0 and g < GROUPS // 2:
                    pe.wait_ge(x_first_half, 16)
                elif g == 0 or isinstance(k, int) and k == 0:
                    pe.wait_ge(x_loaded[u], (q + 1) * 16)
                wait(pe, y_rem_ready, k * GROUPS + g - 1)
                for c in range(CPG):
                    j = g * CPG + c
                    mm = nc.tensor.matmul(y_ps[g % 2][:, c * P:(c + 1) * P], x_sb[u][:, j * P:(j + 1) * P],
                                          w_sel[u % 2][:, :], start=True, stop=True)
                mm.then_inc(y_summed, 1)

            def update(k, u, g):
                if g == 0:
                    pe.wait_ge(bxt_copied, k - 1)
                pe.wait_ge(at_copied, (k - 2) * GROUPS + g + 1)
                wait(pe, z_ready, (k - 2) * GROUPS + g - 1)
                for c in range(CPG):
                    j = g * CPG + c
                    mm = nc.tensor.matmul(z_ps[g % 2][:, c * P:(c + 1) * P], at_sb[u % 2][:, j * P:(j + 1) * P],
                                          bxt_sb[u % 2][:, :], start=True, stop=True)
                mm.then_inc(z_summed, 1)

            def lagged_update(k, q, u, g):
                k2, _, u2, g2 = lagged(k, q, u, g, UPDATE_LAG)
                if live(k2 - 2):
                    update(k2, u2, g2)

            def step(k, q, u):
                for g in range(0, GROUPS, 2):
                    if live(k - 1):
                        project(k, u, g)
                    if live(k - 2) and g == 2:
                        turn_bx(k, u)
                    lagged_update(k, q, u, g)
                    if live(k):
                        main(k, q, u, g)
                        main(k, q, u, g + 1)
                    if live(k - 1):
                        turn_a(k, u, g)
                        project(k, u, g + 1)
                        turn_a(k, u, g + 1)
                    lagged_update(k, q, u, g + 1)

            pe.wait_ge(ident_ready, 2)
            steps(pe, step, 2, BLOCKS, LAST)

        @block.scalar
        def _(act):
            def copy_at(k, u, g):
                wait(act, z_summed, (k - 3) * GROUPS + g + 1)
                act.wait_ge(at_turned, (k - 1) * GROUPS + g + 1)
                nc.scalar.activation(at_sb[(u - 1) % 2][:, g * GW:(g + 1) * GW], at_ps[g % 2][:, 0:GW],
                                     ACT.Copy).then_inc(at_copied, 1)

            def copy_bxt(k, u):
                wait(act, z_summed, (k - 3) * GROUPS)
                act.wait_ge(bxt_turned, k - 1)
                nc.scalar.activation(bxt_sb[u % 2][:, :], bx_ps[u % 2][:, 128:128 + P // 2].bitcast(BF16),
                                     ACT.Copy).then_inc(bxt_copied, 1)

            def copy_y(k, u, g):
                if g == 0:
                    wait(act, z_ready, (k - 3) * GROUPS)
                    wait(act, bx_summed, k - 3)
                act.wait_ge(y_summed, k * GROUPS + g + 1)
                nc.scalar.activation(y_sb[u][:, g * GW:(g + 1) * GW], y_ps[g % 2][:, :],
                                     ACT.Copy).then_inc(y_copied, 1)

            def cast(s, n, source, done):
                nc.scalar.activation(ab_parts[s][:, :, n:NPART:KSLOTS, :].rearrange("p j m r -> p m j r"),
                                     source[:, :, :, :], ACT.Copy).then_inc(done, 1)

            def round_ab(b, q, s, part):
                if part == 1:
                    act.wait_ge(ab_loaded[s], (q + 1) * 16)
                    wait(act, bx_summed, b - 3)
                    wait(act, at_turned, (b - 3) * GROUPS)
                    cast(s, 0, ab_sb[s], ab_part1)
                else:
                    act.wait_ge(ab_rem_ready, b + 1)
                    cast(s, 1, ab_rem, ab_part2)

            def repeat_a(k, u, g):
                parts = ab_parts[u]
                if g == 2:
                    act.wait_ge(a_part3, k + 1)
                    act.wait_ge(ab_part2, k + 1)
                    nc.scalar.activation(parts[:, :, 3:6, :], parts[:, :, 0:3, :], ACT.Copy)
                if g == 3:
                    nc.scalar.activation(parts[:, :, 6:8, :], parts[:, :, 0:2, :], ACT.Copy).then_inc(a_slots_full, 1)

            def step(k, q, u):
                for g in range(0, GROUPS, 2):
                    if live(k):
                        copy_y(k, u, g)
                    if isinstance(k, int) and k == 0 and g == 0:
                        round_ab(0, 0, 0, 2)
                    if live(k + 1) and g == 0:
                        round_ab(k + 1, q + (u + 1) // SLOTS, (u + 1) % SLOTS, 1)
                    if live(k - 2) and g == 2:
                        copy_bxt(k, u)
                    if live(k):
                        copy_y(k, u, g + 1)
                    if live(k - 1):
                        copy_at(k, u, g)
                    if live(k):
                        repeat_a(k, u, g // 2 + 2)
                    if live(k - 1):
                        copy_at(k, u, g + 1)
                    if live(k + 1) and g == 2:
                        round_ab(k + 1, q + (u + 1) // SLOTS, (u + 1) % SLOTS, 2)

            round_ab(0, 0, 0, 1)
            steps(act, step, 1, BLOCKS - 1, LAST)

        @block.vector
        def _(dve):
            def split_bx(k, u, op):
                done = (k - 1) * BX_OPS + op
                if op == 0:
                    dve.wait_ge(bx_summed, k)
                    ins = nc.vector.tensor_reduce(
                        bx[:, :], bx_ps[(u - 1) % 2][:, 0:BX_PARTS * R].rearrange("p (m r) -> p r m", r=R),
                        AX.X, ALU.add)
                else:
                    dve.wait_ge(bx_split, done)
                if op == 1:
                    wait(dve, bxt_turned, k - 1)
                    ins = nc.vector.tensor_copy(bx_parts[:, 0:3, :], bx[:, None, :].broadcast_to((P, 3, R)))
                if op == 2:
                    ins = nc.vector.tensor_tensor(bx_rem[:, :], bx[:, :], bx_parts[:, 0, :], ALU.subtract)
                if op == 3:
                    ins = nc.vector.tensor_copy(bx_parts[:, 3:6, :], bx_rem[:, None, :].broadcast_to((P, 3, R)))
                if op == 4:
                    ins = nc.vector.tensor_tensor(bx_parts[:, 6:8, :], bx_rem[:, None, :].broadcast_to((P, 2, R)),
                                                  bx_parts[:, 3:5, :], ALU.subtract)
                ins.then_inc(bx_split, 1)

            def y_remainder(k, u, g):
                if g == 0:
                    wait(dve, bx_summed, k - 1)
                    wait(dve, y_part3_ready, (k - 1) * GROUPS)
                dve.wait_ge(y_copied, k * GROUPS + g + 1)
                cols = slice(g * GW, (g + 1) * GW)
                upper = slice(2 * g * GW + 1, 2 * (g + 1) * GW, 2)
                nc.vector.tensor_tensor(y_rem[u % 2][:, cols], y_ps[g % 2][:, :], y_sb[u][:, :].bitcast(BF16)[:, upper],
                                        ALU.subtract).then_inc(y_rem_ready, 1)

            def part3_of(k, u, m, slot, done):
                dve.wait_ge(ab_part2, k + 1)
                nc.vector.tensor_tensor(ab_parts[u][:, :, slot, :], ab_rem[:, m, :, :], ab_parts[u][:, :, slot - 1, :],
                                        ALU.subtract).then_inc(done, 1)

            def add_z(k, q, u, g):
                s = (u - 2) % SLOTS
                if g == 0:
                    wait(dve, z_stored[s], turn(q, u, 2) * 16)
                dve.wait_ge(z_summed, (k - 2) * GROUPS + g + 1)
                cols = slice(g * GW, (g + 1) * GW)
                nc.vector.tensor_tensor(z_sb[s][:, cols], z_ps[g % 2][:, :], y_sb[s][:, cols],
                                        ALU.add).then_inc(z_ready, 1)

            def lagged_z(k, q, u, g):
                k2, q2, u2, g2 = lagged(k, q, u, g, UPDATE_LAG)
                if live(k2 - 2):
                    add_z(k2, q2, u2, g2)

            def lagged_split(k, u, op):
                if live(k - 2):
                    split_bx(k - 1, (u - 1) % SLOTS, op)

            def step(k, q, u):
                lagged_split(k, u, 2)
                lagged_z(k, q, u, 0)
                lagged_split(k, u, 3)
                if live(k):
                    y_remainder(k, u, 0)
                lagged_split(k, u, 4)
                if live(k):
                    part3_of(k, u, 0, 2, a_part3)
                    y_remainder(k, u, 1)
                    part3_of(k, u, 1, NPART - 1, b_part3)
                lagged_z(k, q, u, 1)
                lagged_z(k, q, u, 2)
                if live(k):
                    y_remainder(k, u, 2)
                if live(k - 1):
                    split_bx(k, u, 0)
                if live(k):
                    y_remainder(k, u, 3)
                if live(k - 1):
                    split_bx(k, u, 1)
                lagged_z(k, q, u, 3)

            steps(dve, step, 2, BLOCKS, LAST)

        @block.gpsimd
        def _(pool):
            nc.gpsimd.memset(ident_f32[:, :], 0.0).then_inc(zeroed, 1)
            nc.gpsimd.memset(ident_bf16[:, :], 0.0).then_inc(zeroed, 1)
            pool.wait_ge(zeroed, 2)
            for ident in (ident_f32, ident_bf16):
                nc.gpsimd.affine_select(out=ident[:, :], in_=ident[:, :], compare_op=ALU.not_equal, fill=1.0, base=0,
                                        pattern=[[-1, P]], channel_multiplier=1).then_inc(ident_ready, 1)
            pool.wait_ge(ident_ready, 2)

            def select_w(b, m):
                if isinstance(b, int) and b < SLOTS:
                    pool.wait_ge(w_first_loaded[b], 16)
                    chosen = w_first[:, b * C:(b + 1) * C]
                else:
                    if isinstance(b, int) and b == SLOTS:
                        pool.wait_ge(w_table_loaded, 16)
                        pool.wait_ge(cond_loaded, 16)
                    e = pool.value_load(ids_cond[0:1, bass.ds(b, 1)], min_val=0, max_val=EXPERTS - 1)
                    chosen = w_table[:, bass.ds(e * C, C)]
                nc.gpsimd.tensor_tensor(w_sel[m][:, :], chosen, ident_f32[:, :], ALU.add).then_inc(w_ready, 1)

            def remainder_ab(b, s):
                pool.wait_ge(ab_part1, b + 1)
                wait(pool, a_part3, b)
                wait(pool, b_part3, b)
                wait(pool, ab_part2, b)
                nc.gpsimd.tensor_tensor(ab_rem[:, :, :, :], ab_sb[s][:, :, :, :],
                                        ab_parts[s][:, :, 0:NPART:KSLOTS, :].rearrange("p j m r -> p m j r"),
                                        ALU.subtract).then_inc(ab_rem_ready, 1)

            def step(k, q, u):
                for g in range(GROUPS):
                    if g == 1 and (not isinstance(k, int) or live(k + 1)):
                        remainder_ab(k + 1, (u + 1) % SLOTS)
                    pool.wait_ge(y_rem_ready, k * GROUPS + g + 1)
                    if g == 0:
                        wait(pool, bx_summed, k - 1)
                    cols = slice(g * GW, (g + 1) * GW)
                    upper = slice(2 * g * GW + 1, 2 * (g + 1) * GW, 2)
                    nc.gpsimd.tensor_tensor(y_part3[u % 2][:, cols], y_rem[u % 2][:, cols],
                                            y_rem[u % 2][:, :].bitcast(BF16)[:, upper],
                                            ALU.subtract).then_inc(y_part3_ready, 1)
                    if g == 0 and (not isinstance(k, int) or live(k + 1)):
                        wait(pool, y_summed, k * GROUPS)
                        select_w(k + 1, (u + 1) % 2)

            select_w(0, 0)
            remainder_ab(0, 0)
            steps(pool, step, 1, BLOCKS - 1, BATCHES - 1)


def kernel(x, itok_B_0_15, itok_B_4_50, L0_cond_weights, L1_cond_A, L1_cond_B):
    import numpy as np
    import concourse.bacc as bacc
    from concourse.bass_utils import run_bass_kernel_spmd

    x, w = np.asarray(x), np.asarray(L0_cond_weights)
    a, b = np.asarray(L1_cond_A), np.asarray(L1_cond_B)
    batches, c, t = x.shape
    adapters, rank = b.shape[:2]
    chunks = t // P
    a_laid = a.reshape(adapters, chunks, P, rank).transpose(0, 2, 1, 3)
    b_laid = b.reshape(adapters, rank, chunks, P).transpose(0, 3, 2, 1)
    arrays = {
        "x_dram": np.ascontiguousarray(x),
        "cond_dram": np.ascontiguousarray(itok_B_0_15).reshape(1, batches),
        "adapter_dram": np.ascontiguousarray(itok_B_4_50).reshape(1, batches),
        "w_dram": np.ascontiguousarray(w.transpose(1, 0, 2)),
        "ab_dram": np.ascontiguousarray(np.stack([a_laid, b_laid], axis=2)).reshape(adapters, P, -1),
    }
    nc = bacc.Bacc("TRN2", target_bir_lowering=False, num_devices=1)
    ins = [nc.dram_tensor(n, v.shape, mybir.dt.from_np(v.dtype), kind="ExternalInput").ap()
           for n, v in arrays.items()]
    out = nc.dram_tensor("z_dram", (batches, P, t), F32, kind="ExternalOutput").ap()
    build(nc, *ins, out)
    got = run_bass_kernel_spmd(nc, [arrays], core_ids=[0]).results[0]["z_dram"]
    return np.ascontiguousarray(got.reshape(batches, P, chunks, c).transpose(0, 3, 2, 1)).reshape(x.shape)
```
